# Optimizing a Trainium2 kernel written in Bass

```python
import numpy as np
import jax
import jax.numpy as jnp

def _softmax(x, axis=-1):
    return jax.nn.softmax(x, axis=axis)

def _gelu(x):
    return jax.nn.gelu(x, approximate=True)

def _silu(x):
    return jax.nn.silu(x)

def _sigmoid(x):
    return jax.nn.sigmoid(x)

def _layernorm(x, axis=-1, eps=1e-05):
    m = jnp.mean(x, axis=axis, keepdims=True)
    v = jnp.var(x, axis=axis, keepdims=True)
    return (x - m) / jnp.sqrt(v + eps)

def _scatter_add(tgt, idx, src, axis=0):
    return tgt.at[idx].add(src)

def _segment_sum(src, seg, n):
    return jax.ops.segment_sum(src, seg, n)
kernel_name = 'mk_adj_resnorm_d1_adj_r2_6542ea'

def setup_inputs(seed: int=0):
    np.random.seed(seed)
    _w = jnp.asarray

    def _rec_inputs():
        import jax
        import jax.numpy as jnp
        _gk = jax.random.key(seed)
        x = -8.776e-05 + 1 * jax.random.normal(jax.random.fold_in(_gk, 1), (10000, 128), jnp.float32)
        _a = jax.random.bernoulli(jax.random.fold_in(_gk, 2), 0.0002, (10000, 10000))
        _a = jnp.logical_or(_a, jnp.eye(10000, dtype=bool))
        _af = _a.astype(jnp.float32)
        _af = _af * jax.random.uniform(jax.random.fold_in(_gk, 3), (10000, 10000), jnp.float32, 0.05, 1)
        adj = _af
        return (x, adj)
    x, adj = _rec_inputs()

    def _L0_gnn_setup():
        import jax, jax.numpy as jnp
        import numpy as np
        N_USER = 10000
        N_ITEM = 10000
        HID = 128
        key = jax.random.key(seed)
        k1, k2, k3, k4, k5, k6, k7 = jax.random.split(key, 7)
        scale = 1.0 / np.sqrt(HID)
        return {'user_feat': jax.random.normal(k1, (N_USER, HID), dtype=jnp.float32), 'item_feat': jax.random.normal(k2, (N_ITEM, HID), dtype=jnp.float32), 'adj': jax.random.uniform(k3, (N_USER, N_ITEM), dtype=jnp.float32), 'W_item': jax.random.uniform(k4, (HID, HID), dtype=jnp.float32, minval=-scale, maxval=scale), 'b_item': jax.random.uniform(k5, (HID,), dtype=jnp.float32, minval=-scale, maxval=scale), 'W_user': jax.random.uniform(k6, (HID, HID), dtype=jnp.float32, minval=-scale, maxval=scale), 'b_user': jax.random.uniform(k7, (HID,), dtype=jnp.float32, minval=-scale, maxval=scale)}
    _L0_gnn_all = _L0_gnn_setup()
    _L0_gnn_in = {k: v for k, v in _L0_gnn_all.items() if k in ('item_feat', 'W_item', 'b_item', 'W_user', 'b_user')}
    del _L0_gnn_all
    return {'x': x, 'adj': adj, 'L0_gnn_item_feat': _L0_gnn_in['item_feat'], 'L0_gnn_W_item': _L0_gnn_in['W_item'], 'L0_gnn_b_item': _L0_gnn_in['b_item'], 'L0_gnn_W_user': _L0_gnn_in['W_user'], 'L0_gnn_b_user': _L0_gnn_in['b_user']}

def reference(x, adj, L0_gnn_item_feat, L0_gnn_W_item, L0_gnn_b_item, L0_gnn_W_user, L0_gnn_b_user):
    import jax
    import jax.numpy as jnp

    def _L0_gnn_ref(user_feat, item_feat, adj, W_item, b_item, W_user, b_user):
        import jax, jax.numpy as jnp
        import numpy as np
        N_USER = 10000
        N_ITEM = 10000
        HID = 128
        h = item_feat @ W_item.T + b_item
        b = user_feat @ W_user.T + b_user
        return jax.nn.relu(adj @ h + b)
    x = _layernorm(x + _L0_gnn_ref(x, L0_gnn_item_feat, adj, L0_gnn_W_item, L0_gnn_b_item, L0_gnn_W_user, L0_gnn_b_user), axis=-1)
    return x

_drawn_inputs = setup_inputs


def setup_inputs(seed=0):
    import zlib

    import numpy as np

    out = dict(_drawn_inputs(seed))
    spreads = {}
    factors = {}
    for name, (base, spread) in spreads.items():
        noise = np.random.default_rng([zlib.crc32(name.encode()), seed]).standard_normal(out[name].shape)
        drawn = base * np.exp(spread * noise) if base else spread * noise
        out[name] = jnp.asarray(drawn.astype(out[name].dtype))
    for name, factor in factors.items():
        out[name] = (out[name] * factor).astype(out[name].dtype)
    return out
```

```python
from contextlib import ExitStack

import numpy as np

import concourse.bass as bass
from concourse import mybir
from concourse.alu_op_type import AluOpType as ALU

F32 = mybir.dt.float32
F32R = mybir.dt.float32r
ACT = mybir.ActivationFunctionType

USERS, ITEMS, HID, P = 10000, 10000, 128, 128
EPS = 1e-5

GROUPS = 5
GROUP_USERS = USERS // GROUPS
BANK = 512
BANKS = -(-GROUP_USERS // BANK)
WIDTH = [min(BANK, GROUP_USERS - n * BANK) for n in range(BANKS)]

FULL_TILES = ITEMS // P
TAIL = ITEMS - FULL_TILES * P
TAIL_ROWS = 3 * TAIL
LO_ROW = 2 * TAIL
H_TILES = FULL_TILES + 1
GROUP_ROWS = FULL_TILES * P + TAIL_ROWS

TAIL_STEP, X_STEP = FULL_TILES, FULL_TILES + 1
STEPS = FULL_TILES + 2
COUNTED = STEPS - 1
SLOTS = 4
BLOCKS = STEPS // SLOTS
GROUP_START = 0
FIRST_GROUP = 0
FIRST_BATCH = 0
assert STEPS % SLOTS == 0 and TAIL_STEP // SLOTS == BLOCKS - 1

BATCH = BANK // HID
H_BATCHES = -(-H_TILES // BATCH)
CHUNK = 4 * BATCH
CHUNKS = -(-H_TILES // CHUNK)

SUBS = -(-GROUP_USERS // P)
SUB_USERS = [min(P, GROUP_USERS - s * P) for s in range(SUBS)]
SUBS_PER_BANK = BANK // P

STATS_BLOCKS = (2, 3)
MERGE_BLOCK, VAR_BLOCK, RSTD_BLOCK, SHIFT_BLOCK = 4, 5, 6, 7
NORM_BLOCKS = (8, 9)
STORE_BLOCK = 11
WOVEN = 10


def build(nc, adj_T, x_T, item_T, w_item_T, w_user_T, b_item, b_user, out):
    ctx = ExitStack()
    with ctx:
        def sb(name, shape, dtype=F32):
            return ctx.enter_context(nc.sbuf_tensor(name, shape, dtype))

        def sem(name):
            return ctx.enter_context(nc.semaphore(name))

        raw = sb("raw", [P, SLOTS, GROUP_USERS])
        hi = sb("hi", [P, SLOTS, GROUP_USERS], F32R)
        lo = sb("lo", [P, SLOTS, GROUP_USERS], F32R)
        h_hi = sb("h_hi", [P, H_TILES + 1, HID], F32R)
        h_lo = sb("h_lo", [P, H_TILES + 1, HID], F32R)
        h_tail = sb("h_tail", [TAIL_ROWS, HID], F32R)
        h_sum = sb("h_sum", [P, BATCH * HID])
        res = sb("res", [P, GROUP_USERS])
        stage = sb("stage", [P, 2, CHUNK * P])
        relu = stage[:, 0, 0:GROUP_USERS]
        norm = stage[:, 1, 0:SUBS * HID].rearrange("p (s c) -> p s c", c=HID)
        w_item = sb("w_item", [P, HID])
        w_user = sb("w_user", [P, HID])
        b_item_all = sb("b_item_all", [P, HID])
        b_user_col = sb("b_user_col", [HID, 1])
        ident = sb("ident", [P, P])
        stats = sb("stats", [P, SUBS, 6])
        moments = sb("moments", [P, SUBS, 2])
        std = sb("std", [P, SUBS])
        rstd = sb("rstd", [P, SUBS])
        shift = sb("shift", [P, SUBS])

        acc = ctx.enter_context(nc.psum_tensor("acc", [P, BANKS, BANK], F32))
        aux = ctx.enter_context(nc.psum_tensor("aux", [P, BANKS, BANK], F32))

        weights_loaded = sem("weights_loaded")
        biases_loaded = sem("biases_loaded")
        item_loaded = [sem(f"item_loaded{i}") for i in range(2)]
        raw_loaded = [sem(f"raw_loaded{j}") for j in range(SLOTS)]
        ident_ready = sem("ident_ready")
        moments_ready = sem("moments_ready")
        h_psum_done = sem("h_psum_done")
        h_sum_ready = sem("h_sum_ready")
        h_hi_ready = sem("h_hi_ready")
        h_lo_ready = sem("h_lo_ready")
        w_hi_ready = sem("w_hi_ready")
        w_lo_ready = sem("w_lo_ready")
        tail_stacked = sem("tail_stacked")
        hi_ready = sem("hi_ready")
        lo_ready = sem("lo_ready")
        step_done = sem("step_done")
        acc_done = sem("acc_done")
        relu_done = sem("relu_done")
        y_ready = sem("y_ready")
        transposed = sem("transposed")
        stats_taken = sem("stats_taken")
        merged = sem("merged")
        var_ready = sem("var_ready")
        std_ready = sem("std_ready")
        rstd_ready = sem("rstd_ready")
        shift_ready = sem("shift_ready")
        normed = sem("normed")
        out_stored = sem("out_stored")

        block = ctx.enter_context(nc.Block())

        def banks():
            return [(n, slice(n * BANK, n * BANK + WIDTH[n])) for n in range(BANKS)]

        @block.sync
        def _(sp):
            def load_items(c):
                lo_tile, hi_tile = c * CHUNK, min((c + 1) * CHUNK, H_TILES)
                sp.dma_start(stage[:, c % 2, 0:(hi_tile - lo_tile) * P],
                             item_T[:, lo_tile * P:hi_tile * P]).then_inc(item_loaded[c % 2], 16)

            def load_step(g, b, j, rows=P, first=False):
                if not first:
                    sp.wait_ge(lo_ready, g * STEPS + b * SLOTS + (j - SLOTS + 1))
                row = g * GROUP_ROWS + b * (SLOTS * P) + j * P
                sp.dma_start(raw[0:rows, j, :], adj_T[bass.ds(row, rows), :]).then_inc(raw_loaded[j], 16)

            def load_block(g, b, first=False):
                for j in range(SLOTS):
                    load_step(g, b, j, first=first)

            def load_last_block(g):
                b = BLOCKS - 1
                for j in range(SLOTS - 2):
                    load_step(g, b, j)
                load_step(g, b, SLOTS - 2, rows=TAIL_ROWS)
                sp.wait_ge(lo_ready, g * STEPS + (X_STEP - SLOTS + 1))
                sp.dma_start(raw[:, SLOTS - 1, :], x_T[bass.ds(g * P, P), :]).then_inc(raw_loaded[SLOTS - 1], 16)

            def store(e):
                sp.wait_ge(normed, e + 1)
                whole = SUBS - 1
                rows = out[bass.ds(e * GROUP_USERS, whole * P), :].rearrange("(s p) c -> p s c", p=P)
                sp.dma_start(rows, norm[:, 0:whole, :]).then_inc(out_stored, 16)
                sp.dma_start(out[bass.ds(e * GROUP_USERS + whole * P, SUB_USERS[whole]), :],
                             norm[0:SUB_USERS[whole], whole, :]).then_inc(out_stored, 16)

            load_items(0)
            load_block(0, 0, first=True)
            load_items(1)
            for c in range(2, CHUNKS):
                start = 1 if c == 2 else 4 * (c - 2)
                with sp.Fori(start, 4 * (c - 1)) as b:
                    load_block(0, b)
                sp.wait_ge(h_psum_done, 4 * (c - 1))
                load_items(c)
            with sp.Fori(4 * (CHUNKS - 2), BLOCKS - 1) as b:
                load_block(0, b)
            load_last_block(0)

            with sp.Fori(1, GROUPS) as g:
                with sp.Fori(0, STORE_BLOCK) as b:
                    load_block(g, b)
                store(g - 1)
                with sp.Fori(STORE_BLOCK, BLOCKS - 1) as b:
                    load_block(g, b)
                load_last_block(g)
            store(GROUPS - 1)
            sp.wait_ge(out_stored, 32 * GROUPS)

        @block.gpsimd
        def _(pool):
            pool.dma_start(b_item_all[:, :], b_item.partition_broadcast(P)).then_inc(biases_loaded, 16)
            pool.dma_start(b_user_col[:, :], b_user).then_inc(biases_loaded, 16)
            pool.memset(ident[:, :], 0.0).then_inc(ident_ready, 1)
            pool.wait_ge(ident_ready, 1)
            pool.affine_select(out=ident[:, :], in_=ident[:, :], compare_op=ALU.not_equal, fill=1.0,
                               base=0, pattern=[[-1, P]], channel_multiplier=1).then_inc(ident_ready, 1)
            pool.wait_ge(h_lo_ready, H_BATCHES)
            for row, part in ((0, h_hi), (TAIL, h_lo), (2 * TAIL, h_hi)):
                pool.dma_start(h_tail[row:row + TAIL, :], part[0:TAIL, FULL_TILES, :]).then_inc(tail_stacked, 16)

        @block.scalar
        def _(act):
            def round_step(g, b, j, rows=P, first=False):
                act.wait_ge(raw_loaded[j], g * (16 * BLOCKS) + b * 16 + 16)
                if b is not GROUP_START:
                    act.wait_ge(step_done, g * COUNTED + b * SLOTS + (j - SLOTS + 1))
                elif not first and j < SLOTS - 1:
                    act.wait_ge(step_done, g * COUNTED + (j - SLOTS + 2))
                act.activation(hi[0:rows, j, :], raw[0:rows, j, :], ACT.Copy).then_inc(hi_ready, 1)

            def round_block(g, b, first=False):
                for j in range(SLOTS):
                    round_step(g, b, j, first=first)

            def round_last_block(g):
                b = BLOCKS - 1
                for j in range(SLOTS - 2):
                    round_step(g, b, j)
                round_step(g, b, SLOTS - 2, rows=TAIL_ROWS)
                act.wait_ge(raw_loaded[SLOTS - 1], g * (16 * BLOCKS) + 16 * BLOCKS)
                act.wait_ge(step_done, g * COUNTED + (X_STEP - SLOTS + 1))
                act.activation(res[:, :], raw[:, SLOTS - 1, :], ACT.Copy)
                round_step(g, b, SLOTS - 1)

            def round_h(q, tiles=BATCH):
                act.wait_ge(h_sum_ready, q + 1)
                act.activation(h_hi[:, bass.ds(q * BATCH, tiles), :].rearrange("p t c -> p (t c)"),
                               h_sum[:, 0:tiles * HID], ACT.Copy).then_inc(h_hi_ready, 1)

            def relus(e):
                for n, cols in banks():
                    act.wait_ge(acc_done, e * BANKS + n + 1)
                    act.activation(relu[:, cols], acc[:, n, 0:WIDTH[n]], ACT.Relu,
                                   bias=b_user_col[:, 0:1]).then_inc(relu_done, 1)

            def take_root(e):
                act.wait_ge(var_ready, e + 1)
                act.activation(std[:, :], rstd[:, :], ACT.Sqrt).then_inc(std_ready, 1)

            def normalise(e, subs):
                if subs[0] == 0:
                    act.wait_ge(shift_ready, e + 1)
                    act.wait_ge(out_stored, 32 * e)
                for s in subs:
                    n, users = s // SUBS_PER_BANK, SUB_USERS[s]
                    col = (s % SUBS_PER_BANK) * P
                    done = act.activation(norm[0:users, s, :], aux[0:users, n, col:col + HID], ACT.Identity,
                                          bias=shift[0:users, s:s + 1], scale=rstd[0:users, s:s + 1])
                if s == SUBS - 1:
                    done.then_inc(normed, 1)

            act.dma_start(w_item[:, :], w_item_T).then_inc(weights_loaded, 16)
            act.dma_start(w_user[:, :], w_user_T).then_inc(weights_loaded, 16)
            act.preload_act_table(ACT.Sqrt)
            act.wait_ge(weights_loaded, 32)
            act.wait_ge(biases_loaded, 32)
            act.activation(h_hi[:, H_TILES, :], w_user[:, :], ACT.Copy).then_inc(w_hi_ready, 1)

            def round_block_and_h(b, first=False, tiles=BATCH):
                for j in range(SLOTS):
                    if j == SLOTS // 2:
                        round_h(b + 1, tiles)
                    round_step(0, b, j, first=first)

            round_h(0)
            round_block_and_h(0, first=True)
            with act.Fori(1, BLOCKS - 2) as b:
                round_block_and_h(b)
            round_block_and_h(BLOCKS - 2, tiles=H_TILES - (H_BATCHES - 1) * BATCH)
            round_last_block(0)

            with act.Fori(1, GROUPS) as g:
                e = g - 1
                for b in range(WOVEN):
                    for j in range(SLOTS):
                        if b == 0 and j == SLOTS - 1:
                            relus(e)
                        if b == VAR_BLOCK and j == SLOTS // 2:
                            take_root(e)
                        if b in NORM_BLOCKS and j == 0:
                            half = NORM_BLOCKS.index(b)
                            normalise(e, range(half * SUBS // 2, (half + 1) * SUBS // 2))
                        round_step(g, b, j)
                with act.Fori(WOVEN, BLOCKS - 1) as b:
                    round_block(g, b)
                round_last_block(g)

            relus(GROUPS - 1)
            take_root(GROUPS - 1)
            normalise(GROUPS - 1, range(SUBS))

        @block.vector
        def _(dve):
            def subtract_step(g, b, j):
                dve.wait_ge(hi_ready, g * STEPS + b * SLOTS + (j + 1))
                dve.tensor_tensor(lo[:, j, :], raw[:, j, :], hi[:, j, :].bitcast(F32),
                                  ALU.subtract).then_inc(lo_ready, 1)

            def subtract_block(g, b):
                for j in range(SLOTS):
                    subtract_step(g, b, j)

            def subtract_last_block(g):
                b = BLOCKS - 1
                for j in range(SLOTS - 2):
                    subtract_step(g, b, j)
                dve.wait_ge(hi_ready, g * STEPS + (TAIL_STEP + 1))
                third = slice(LO_ROW, LO_ROW + TAIL)
                dve.tensor_tensor(hi[third, SLOTS - 2, :], raw[third, SLOTS - 2, :],
                                  hi[third, SLOTS - 2, :].bitcast(F32), ALU.subtract).then_inc(lo_ready, 1)
                subtract_step(g, b, SLOTS - 1)

            def add_bias(q, bank, tiles=BATCH):
                if q is not FIRST_BATCH:
                    dve.wait_ge(h_lo_ready, q)
                dve.wait_ge(h_psum_done, q + 1)
                dve.tensor_tensor(h_sum[:, 0:tiles * HID].rearrange("p (t c) -> p t c", c=HID),
                                  aux[:, bank, 0:tiles * HID].rearrange("p (t c) -> p t c", c=HID),
                                  b_item_all[:, :].unsqueeze(1).to_broadcast([P, tiles, HID]),
                                  ALU.add).then_inc(h_sum_ready, 1)

            def subtract_h(q, tiles=BATCH):
                dve.wait_ge(h_hi_ready, q + 1)
                part = (slice(None), bass.ds(q * BATCH, tiles), slice(None))
                dve.tensor_tensor(h_lo[part].rearrange("p t c -> p (t c)"), h_sum[:, 0:tiles * HID],
                                  h_hi[part].rearrange("p t c -> p (t c)").bitcast(F32),
                                  ALU.subtract).then_inc(h_lo_ready, 1)

            def add_residual(e):
                for n, cols in banks():
                    dve.wait_ge(relu_done, e * BANKS + n + 1)
                    dve.tensor_tensor(res[:, cols], relu[:, cols], res[:, cols], ALU.add).then_inc(y_ready, 1)

            def take_stats(e, bank_list):
                for n in bank_list:
                    dve.wait_ge(transposed, e * BANKS + n + 1)
                    for s in range(n * SUBS_PER_BANK, (n + 1) * SUBS_PER_BANK):
                        users, col = SUB_USERS[s], (s % SUBS_PER_BANK) * P
                        done = dve.bn_stats(stats[0:users, s, :], aux[0:users, n, col:col + HID])
                    done.then_inc(stats_taken, 1)

            def await_stats(e):
                dve.wait_ge(stats_taken, (e + 1) * BANKS)

            def merge_stats(e):
                for s in range(SUBS):
                    done = dve.bn_aggr(moments[0:SUB_USERS[s], s, :], stats[0:SUB_USERS[s], s, :])
                done.then_inc(merged, 1)

            def guard_variance(e):
                dve.wait_ge(merged, e + 1)
                dve.tensor_scalar(rstd[:, :], moments[:, :, 1], EPS, None, ALU.add).then_inc(var_ready, 1)

            def invert_std(e):
                dve.wait_ge(std_ready, e + 1)
                dve.reciprocal(rstd[:, :], std[:, :]).then_inc(rstd_ready, 1)

            def make_shift(e):
                dve.wait_ge(rstd_ready, e + 1)
                dve.scalar_tensor_tensor(out=shift[:, :], in0=moments[:, :, 0], scalar=-1.0, in1=rstd[:, :],
                                         op0=ALU.mult, op1=ALU.mult).then_inc(shift_ready, 1)

            dve.memset(moments[:, :, :], 1.0).then_inc(moments_ready, 1)
            dve.wait_ge(moments_ready, 1)
            dve.wait_ge(w_hi_ready, 1)
            dve.wait_ge(biases_loaded, 32)
            dve.tensor_tensor(h_lo[:, H_TILES, :], w_user[:, :], h_hi[:, H_TILES, :].bitcast(F32),
                              ALU.subtract).then_inc(w_lo_ready, 1)

            def subtract_block_and_h(b, bank, tiles=BATCH):
                for j in range(SLOTS):
                    if j == 0:
                        add_bias(b + 1, bank, tiles)
                    if j == SLOTS // 2:
                        subtract_h(b + 1, tiles)
                    subtract_step(0, b, j)

            add_bias(FIRST_BATCH, 0)
            subtract_h(FIRST_BATCH)
            with dve.Fori(0, BLOCKS - 2, 2) as b:
                subtract_block_and_h(b, 1)
                subtract_block_and_h(b + 1, 0)
            subtract_block_and_h(BLOCKS - 2, 1, tiles=H_TILES - (H_BATCHES - 1) * BATCH)
            subtract_last_block(0)

            with dve.Fori(1, GROUPS) as g:
                e = g - 1
                for b in range(WOVEN):
                    if b in STATS_BLOCKS:
                        half = STATS_BLOCKS.index(b)
                        take_stats(e, range(half * BANKS // 2, (half + 1) * BANKS // 2))
                    if b == MERGE_BLOCK:
                        await_stats(e)
                    if b == VAR_BLOCK:
                        guard_variance(e)
                    if b == RSTD_BLOCK:
                        invert_std(e)
                    if b == SHIFT_BLOCK:
                        make_shift(e)
                    for j in range(SLOTS):
                        if b == 0 and j == SLOTS - 1:
                            add_residual(e)
                        subtract_step(g, b, j)
                        if b == MERGE_BLOCK and j == 0:
                            merge_stats(e)
                with dve.Fori(WOVEN, BLOCKS - 1) as b:
                    subtract_block(g, b)
                subtract_last_block(g)

            e = GROUPS - 1
            add_residual(e)
            take_stats(e, range(BANKS))
            await_stats(e)
            merge_stats(e)
            guard_variance(e)
            invert_std(e)
            make_shift(e)

        @block.tensor
        def _(pe):
            def multiply_h(q):
                chunk = q * BATCH // CHUNK
                if q * BATCH % CHUNK == 0:
                    pe.wait_ge(item_loaded[chunk % 2], 16 * (chunk // 2 + 1))
                if q >= 2:
                    pe.wait_ge(h_sum_ready, q - 1)
                for t in range(q * BATCH, min((q + 1) * BATCH, H_TILES)):
                    at = (t - chunk * CHUNK) * P
                    done = pe.matmul(aux[:, q % 2, (t % BATCH) * HID:(t % BATCH + 1) * HID],
                                     stage[:, chunk % 2, at:at + P], w_item[:, :], start=True, stop=True)
                done.then_inc(h_psum_done, 1)

            def multiply(n, j, weights, moving, start=False, stop=False, rows=P):
                return pe.matmul(acc[:, n, 0:WIDTH[n]], weights, moving[0:rows, j, n * BANK:n * BANK + WIDTH[n]],
                                 start=start, stop=stop)

            def multiply_step(g, k):
                j = k % SLOTS
                count = g * STEPS + (k + 1)
                w_hi, w_lo = h_hi[:, k, :], h_lo[:, k, :]
                if 0 < k < FULL_TILES:
                    pe.wait_ge(hi_ready, count)
                    for n in range(BANKS):
                        multiply(n, j, w_hi, hi)
                    for n in range(BANKS):
                        multiply(n, j, w_lo, hi)
                    pe.wait_ge(lo_ready, count)
                    for n in range(BANKS):
                        done = multiply(n, j, w_hi, lo)
                elif k == TAIL_STEP:
                    pe.wait_ge(lo_ready, count)
                    for n in range(BANKS):
                        done = multiply(n, j, h_tail[:, :], hi, rows=TAIL_ROWS)
                else:
                    pe.wait_ge(lo_ready, count)
                    for n in range(BANKS):
                        if k == 0 and g is not FIRST_GROUP:
                            pe.wait_ge(relu_done, g * BANKS + (n - BANKS + 1))
                        multiply(n, j, w_hi, hi, start=(k == 0))
                        multiply(n, j, w_lo, hi)
                        done = multiply(n, j, w_hi, lo, stop=(k == X_STEP))
                        if k == X_STEP:
                            done.then_inc(acc_done, 1)
                if k != X_STEP:
                    done.then_inc(step_done, 1)

            def transpose_banks(e):
                for n in range(BANKS):
                    pe.wait_ge(y_ready, e * BANKS + n + 1)
                    for s in range(n * SUBS_PER_BANK, (n + 1) * SUBS_PER_BANK):
                        users, col = SUB_USERS[s], (s % SUBS_PER_BANK) * P
                        done = pe.transpose(aux[0:users, n, col:col + HID], res[:, s * P:s * P + users], ident[:, :])
                    done.then_inc(transposed, 1)

            pe.wait_ge(weights_loaded, 32)
            pe.wait_ge(ident_ready, 2)
            multiply_h(0)
            multiply_h(1)
            for k in range(STEPS):
                if k % SLOTS == 0:
                    if k // SLOTS + 2 < H_BATCHES:
                        multiply_h(k // SLOTS + 2)
                    pe.wait_ge(h_lo_ready, min(k // SLOTS + 1, H_BATCHES))
                if k == TAIL_STEP:
                    pe.wait_ge(tail_stacked, 48)
                if k == X_STEP:
                    pe.wait_ge(w_lo_ready, 1)
                multiply_step(FIRST_GROUP, k)

            with pe.Fori(1, GROUPS) as g:
                for k in range(STEPS):
                    if k == SLOTS:
                        if_first = g - 1
                        transpose_banks(if_first)
                    multiply_step(g, k)
            transpose_banks(GROUPS - 1)


def kernel(x, adj, L0_gnn_item_feat, L0_gnn_W_item, L0_gnn_b_item, L0_gnn_W_user, L0_gnn_b_user):
    import concourse.bacc as bacc
    from concourse.bass_utils import run_bass_kernel_spmd

    def by_group(a_T):
        rows = a_T.shape[0]
        return np.ascontiguousarray(a_T.reshape(rows, GROUPS, GROUP_USERS).transpose(1, 0, 2)).reshape(
            GROUPS * rows, GROUP_USERS)

    adj_T = np.asarray(adj).T
    tail = adj_T[FULL_TILES * P:]
    item_T = np.zeros((HID, H_TILES * P), np.asarray(L0_gnn_item_feat).dtype)
    item_T[:, :ITEMS] = np.asarray(L0_gnn_item_feat).T
    arrays = {
        "adj_T": by_group(np.concatenate([adj_T, tail, tail])),
        "x_T": by_group(np.ascontiguousarray(np.asarray(x).T)),
        "item_T": item_T,
        "w_item_T": np.ascontiguousarray(np.asarray(L0_gnn_W_item).T),
        "w_user_T": np.ascontiguousarray(np.asarray(L0_gnn_W_user).T),
        "b_item": np.asarray(L0_gnn_b_item),
        "b_user": np.asarray(L0_gnn_b_user).reshape(HID, 1),
    }
    nc = bacc.Bacc("TRN2", target_bir_lowering=False, num_devices=1)
    ins = [nc.dram_tensor(name, a.shape, mybir.dt.from_np(a.dtype), kind="ExternalInput").ap()
           for name, a in arrays.items()]
    out = nc.dram_tensor("out", (USERS, HID), F32, kind="ExternalOutput").ap()
    build(nc, *ins, out)
    result = run_bass_kernel_spmd(nc, [arrays], core_ids=[0])
    return result.results[0]["out"]
```

```python
from contextlib import ExitStack

import numpy as np

import concourse.bass as bass
from concourse import mybir
from concourse.alu_op_type import AluOpType as ALU

F32 = mybir.dt.float32
F32R = mybir.dt.float32r
ACT = mybir.ActivationFunctionType

USERS, ITEMS, HID, P = 10000, 10000, 128, 128
EPS = 1e-5

GROUPS = 5
GROUP_USERS = USERS // GROUPS
PITCH = -(-GROUP_USERS // 64) * 64
BANK = 512
BANKS = -(-GROUP_USERS // BANK)
WIDTH = [min(BANK, GROUP_USERS - n * BANK) for n in range(BANKS)]

TAIL = 32
TAIL_ROWS = 3 * TAIL
TILES = -(-(ITEMS - TAIL) // P)
SHORT = ITEMS - TAIL - (TILES - 1) * P
H_TILES = TILES + 1

STEPS = TILES + 2
COUNTED = STEPS - 1
SLOTS = 4
BLOCKS = STEPS // SLOTS
GROUP_START = 0
FIRST_GROUP = 0
FIRST_BATCH = 0
SPECIAL = BLOCKS - 2
TAIL_SLOT, X_SLOT = 1, 2
TAIL_STEP, X_STEP = SPECIAL * SLOTS + TAIL_SLOT, SPECIAL * SLOTS + X_SLOT
LAST_SLOT, LAST_STEP = SLOTS - 1, STEPS - 1
assert STEPS % SLOTS == 0

BATCH = BANK // HID
H_BATCHES = -(-H_TILES // BATCH)
LAST_BATCH = H_TILES - (H_BATCHES - 1) * BATCH
CHUNK = 4 * BATCH
CHUNKS = -(-H_TILES // CHUNK)

SUBS = -(-GROUP_USERS // P)
SUB_USERS = [min(P, GROUP_USERS - s * P) for s in range(SUBS)]
SUBS_PER_BANK = BANK // P

HALF_BANKS = BANKS // 2
HALF_SUBS = SUBS // 2

STATS_BLOCKS = (2, 3)
MERGE_BLOCKS = (4, 5)
RSTD_BLOCKS = (6, 7)
NORM_BLOCKS = (8, 9)
WOVEN = 10
STORE_BLOCK = 11


def build(nc, adj_T, x_T, item_T, w_item_T, w_user_T, b_item, b_user, out):
    ctx = ExitStack()
    with ctx:
        def sb(name, shape, dtype=F32):
            return ctx.enter_context(nc.sbuf_tensor(name, shape, dtype))

        def sem(name):
            return ctx.enter_context(nc.semaphore(name))

        raw = sb("raw", [P, SLOTS, GROUP_USERS])
        hi = sb("hi", [P, SLOTS, GROUP_USERS], F32R)
        lo = sb("lo", [P, SLOTS, GROUP_USERS], F32R)
        h_hi = sb("h_hi", [P, H_TILES + 1, HID], F32R)
        h_lo = sb("h_lo", [P, H_TILES + 1, HID], F32R)
        h_tail = sb("h_tail", [TAIL_ROWS, HID], F32R)
        h_sum = sb("h_sum", [P, BATCH * HID])
        res = sb("res", [P, GROUP_USERS])
        stage = sb("stage", [P, 2, CHUNK * P])
        relu = stage[:, 0, 0:GROUP_USERS]
        norm = stage[:, 1, 0:SUBS * HID].rearrange("p (s c) -> p s c", c=HID)
        w_item = sb("w_item", [P, HID])
        w_user = sb("w_user", [P, HID])
        b_item_all = sb("b_item_all", [P, HID])
        b_user_col = sb("b_user_col", [HID, 1])
        ident = sb("ident", [P, P])
        eps_col = sb("eps_col", [P, 1])
        stats = sb("stats", [P, SUBS, 6])
        moments = sb("moments", [P, SUBS, 2])
        std = sb("std", [P, SUBS])
        guess = sb("guess", [P, SUBS])
        check = sb("check", [P, SUBS])
        rstd = sb("rstd", [P, SUBS])
        shift = sb("shift", [P, SUBS])

        acc = ctx.enter_context(nc.psum_tensor("acc", [P, BANKS, BANK], F32))
        aux = ctx.enter_context(nc.psum_tensor("aux", [P, BANKS, BANK], F32))

        weights_loaded = sem("weights_loaded")
        biases_loaded = sem("biases_loaded")
        item_first_loaded = sem("item_first_loaded")
        item_loaded = [sem(f"item_loaded{i}") for i in range(2)]
        raw_loaded = [sem(f"raw_loaded{j}") for j in range(SLOTS)]
        ident_ready = sem("ident_ready")
        fills_ready = sem("fills_ready")
        h_psum_done = sem("h_psum_done")
        h_sum_ready = sem("h_sum_ready")
        h_hi_ready = sem("h_hi_ready")
        h_lo_ready = sem("h_lo_ready")
        w_hi_ready = sem("w_hi_ready")
        w_lo_ready = sem("w_lo_ready")
        h_tail_ready = sem("h_tail_ready")
        hi_ready = sem("hi_ready")
        lo_ready = sem("lo_ready")
        last_hi_ready = sem("last_hi_ready")
        last_lo_ready = sem("last_lo_ready")
        step_done = sem("step_done")
        acc_done = sem("acc_done")
        relu_done = sem("relu_done")
        y_ready = sem("y_ready")
        y_too_ready = sem("y_too_ready")
        transposed = sem("transposed")
        stats_taken = sem("stats_taken")
        merged = sem("merged")
        std_ready = sem("std_ready")
        guess_ready = sem("guess_ready")
        check_ready = sem("check_ready")
        rstd_ready = sem("rstd_ready")
        shift_ready = sem("shift_ready")
        normed = sem("normed")
        normed_too = sem("normed_too")
        out_stored = sem("out_stored")

        block = ctx.enter_context(nc.Block())

        def banks():
            return [(n, slice(n * BANK, n * BANK + WIDTH[n])) for n in range(BANKS)]

        @block.sync
        def _(sp):
            def load_items(c, skip=0):
                first, end = c * CHUNK + skip, min((c + 1) * CHUNK, H_TILES)
                sp.dma_start(stage[:, c % 2, skip * P:(end - c * CHUNK) * P],
                             item_T[:, first * P:end * P]).then_inc(item_loaded[c % 2], 16)

            def load(g, b, j):
                row = g * ITEMS + b * (SLOTS * P) + j * P
                sp.dma_start(raw[:, j, :], adj_T[bass.ds(row, P), 0:GROUP_USERS]).then_inc(raw_loaded[j], 16)

            def load_start(g):
                for j in range(SLOTS - 1):
                    sp.wait_ge(lo_ready, g * COUNTED + (j - SLOTS + 2))
                    load(g, GROUP_START, j)
                sp.wait_ge(last_lo_ready, g * BANKS)
                load(g, GROUP_START, SLOTS - 1)

            def load_block(g, b):
                for j in range(SLOTS):
                    sp.wait_ge(lo_ready, g * COUNTED + b * SLOTS + (j - SLOTS + 1))
                    load(g, b, j)

            def load_last_blocks(g):
                for k in range(SPECIAL * SLOTS, STEPS):
                    j = k % SLOTS
                    sp.wait_ge(lo_ready, g * COUNTED + (k - SLOTS + 1))
                    if k == X_STEP:
                        source, rows = x_T[bass.ds(g * P, P), 0:GROUP_USERS], P
                    elif k == TAIL_STEP:
                        source, rows = adj_T[bass.ds(g * ITEMS + (ITEMS - TAIL), TAIL), 0:GROUP_USERS], TAIL
                    else:
                        rows = SHORT if k == LAST_STEP else P
                        first = (k if k < TAIL_STEP else k - 2) * P
                        source = adj_T[bass.ds(g * ITEMS + first, rows), 0:GROUP_USERS]
                    sp.dma_start(raw[0:rows, j, :], source).then_inc(raw_loaded[j], 16)

            def store(e, first, end):
                whole = min(end, SUBS - 1)
                rows = out[bass.ds(e * GROUP_USERS + first * P, (whole - first) * P), :]
                sp.dma_start(rows.rearrange("(s p) c -> p s c", p=P), norm[:, first:whole, :]
                             ).then_inc(out_stored, 16)
                if whole < end:
                    sp.dma_start(out[bass.ds(e * GROUP_USERS + whole * P, SUB_USERS[whole]), :],
                                 norm[0:SUB_USERS[whole], whole, :]).then_inc(out_stored, 16)

            sp.dma_start(stage[:, 0, 0:BATCH * P], item_T[:, 0:BATCH * P]).then_inc(item_first_loaded, 16)
            load(FIRST_GROUP, 0, 0)
            load_items(0, skip=BATCH)
            for j in range(1, SLOTS):
                load(FIRST_GROUP, 0, j)
            load_items(1)
            for c in range(2, CHUNKS):
                with sp.Fori(1 if c == 2 else 4 * (c - 2), 4 * (c - 1)) as b:
                    load_block(0, b)
                sp.wait_ge(h_psum_done, 4 * (c - 1))
                load_items(c)
            with sp.Fori(4 * (CHUNKS - 2), SPECIAL) as b:
                load_block(0, b)
            load_last_blocks(0)

            with sp.Fori(1, GROUPS) as g:
                load_start(g)
                with sp.Fori(1, STORE_BLOCK) as b:
                    load_block(g, b)
                sp.wait_ge(normed, g * 2)
                store(g - 1, 0, SUBS)
                with sp.Fori(STORE_BLOCK, SPECIAL) as b:
                    load_block(g, b)
                load_last_blocks(g)

            e = GROUPS - 1
            for half in range(2):
                sp.wait_ge(normed, e * 2 + half + 1)
                if half == 1:
                    sp.wait_ge(normed_too, 1)
                store(e, half * HALF_SUBS, (half + 1) * HALF_SUBS)
            sp.wait_ge(out_stored, 32 * e + 16 * 3)

        @block.gpsimd
        def _(pool):
            pool.dma_start(b_item_all[:, :], b_item.partition_broadcast(P)).then_inc(biases_loaded, 16)
            pool.dma_start(b_user_col[:, :], b_user).then_inc(biases_loaded, 16)
            pool.memset(ident[:, :], 0.0).then_inc(ident_ready, 1)
            pool.wait_ge(ident_ready, 1)
            pool.affine_select(out=ident[:, :], in_=ident[:, :], compare_op=ALU.not_equal, fill=1.0,
                               base=0, pattern=[[-1, P]], channel_multiplier=1).then_inc(ident_ready, 1)

            def add_residual(e, of_banks):
                for n, cols in of_banks:
                    pool.wait_ge(relu_done, e * BANKS + n + 1)
                    pool.tensor_tensor(res[:, cols], relu[:, cols], res[:, cols], ALU.add).then_inc(y_ready, 1)

            with pool.Fori(1, GROUPS) as g:
                add_residual(g - 1, banks())
            add_residual(GROUPS - 1, (banks()[0], banks()[-1]))

        @block.scalar
        def _(act):
            def round_tile(g, b, j, rows=P):
                act.wait_ge(raw_loaded[j], g * (16 * BLOCKS) + b * 16 + 16)
                act.activation(hi[0:rows, j, :], raw[0:rows, j, :], ACT.Copy).then_inc(hi_ready, 1)

            def round_step(g, b, j, rows=P):
                act.wait_ge(step_done, g * COUNTED + b * SLOTS + (j - SLOTS + 1))
                round_tile(g, b, j, rows)

            def round_special_block(g, between=lambda: None):
                round_step(g, SPECIAL, 0)
                round_step(g, SPECIAL, TAIL_SLOT, rows=TAIL)
                between()
                act.wait_ge(raw_loaded[X_SLOT], g * (16 * BLOCKS) + 16 * (SPECIAL + 1))
                act.activation(res[:, :], raw[:, X_SLOT, :], ACT.Copy)
                round_step(g, SPECIAL, X_SLOT)
                round_step(g, SPECIAL, LAST_SLOT)

            def round_last_block(g):
                for j in range(LAST_SLOT):
                    round_step(g, BLOCKS - 1, j)
                act.wait_ge(step_done, g * COUNTED + (LAST_STEP - SLOTS + 1))
                act.wait_ge(raw_loaded[LAST_SLOT], g * (16 * BLOCKS) + 16 * BLOCKS)
                for n, cols in banks():
                    act.activation(hi[0:SHORT, LAST_SLOT, cols], raw[0:SHORT, LAST_SLOT, cols],
                                   ACT.Copy).then_inc(last_hi_ready, 1)

            def round_h(q, tiles=BATCH):
                act.wait_ge(h_sum_ready, q + 1)
                act.activation(h_hi[:, bass.ds(q * BATCH, tiles), :].rearrange("p t c -> p (t c)"),
                               h_sum[:, 0:tiles * HID], ACT.Copy).then_inc(h_hi_ready, 1)

            def relus(e):
                for n, cols in banks():
                    act.wait_ge(acc_done, e * BANKS + n + 1)
                    act.activation(relu[:, cols], acc[:, n, 0:WIDTH[n]], ACT.Relu,
                                   bias=b_user_col[:, 0:1]).then_inc(relu_done, 1)

            def take_root(e, half):
                act.wait_ge(merged, e * 2 + half + 1)
                subs = slice(half * HALF_SUBS, (half + 1) * HALF_SUBS)
                act.activation(std[:, subs], moments[:, subs, 1], ACT.Sqrt, bias=eps_col[:, 0:1]
                               ).then_inc(std_ready, 1)

            def normalise(e, half, of_banks=range(HALF_BANKS)):
                act.wait_ge(shift_ready, e * 2 + half + 1)
                first = half * HALF_SUBS
                for s in range(first + of_banks[0] * SUBS_PER_BANK, first + (of_banks[-1] + 1) * SUBS_PER_BANK):
                    n, users, col = s // SUBS_PER_BANK, SUB_USERS[s], (s % SUBS_PER_BANK) * P
                    done = act.activation(norm[0:users, s, :], aux[0:users, n, col:col + HID], ACT.Identity,
                                          bias=shift[0:users, s:s + 1], scale=rstd[0:users, s:s + 1])
                if half == 1 or of_banks[-1] == HALF_BANKS - 1:
                    done.then_inc(normed, 1)

            act.dma_start(w_item[:, :], w_item_T).then_inc(weights_loaded, 16)
            act.dma_start(w_user[:, :], w_user_T).then_inc(weights_loaded, 16)
            act.preload_act_table(ACT.Sqrt)
            act.wait_ge(weights_loaded, 32)
            act.wait_ge(biases_loaded, 32)
            act.activation(h_hi[:, H_TILES, :], w_user[:, :], ACT.Copy).then_inc(w_hi_ready, 1)

            def round_block_and_h(b, round_one=round_step, tiles=BATCH):
                for j in range(SLOTS):
                    if j == SLOTS // 2:
                        round_h(b + 1, tiles)
                    round_one(0, b, j)

            round_h(0)
            round_block_and_h(0, round_one=round_tile)
            with act.Fori(1, SPECIAL) as b:
                round_block_and_h(b)
            act.wait_ge(h_lo_ready, TAIL_STEP // BATCH + 1)
            for part, source in enumerate((h_hi, h_hi, h_lo)):
                done = act.activation(h_tail[part * TAIL:(part + 1) * TAIL, :],
                                      source[0:TAIL, TAIL_STEP, :].bitcast(F32), ACT.Copy)
            done.then_inc(h_tail_ready, 1)
            round_special_block(0, between=lambda: round_h(H_BATCHES - 1, LAST_BATCH))
            round_last_block(0)

            act.wait_ge(fills_ready, 2)
            with act.Fori(1, GROUPS) as g:
                e = g - 1
                for j in range(LAST_SLOT):
                    act.wait_ge(step_done, g * COUNTED + (j - SLOTS + 2))
                    round_tile(g, GROUP_START, j)
                    if j == 0:
                        relus(e)
                round_tile(g, GROUP_START, LAST_SLOT)
                for b in range(1, WOVEN):
                    for j in range(SLOTS):
                        if b in MERGE_BLOCKS and j == SLOTS // 2:
                            take_root(e, MERGE_BLOCKS.index(b))
                        if b in NORM_BLOCKS and j == 0:
                            normalise(e, NORM_BLOCKS.index(b))
                        round_step(g, b, j)
                with act.Fori(WOVEN, SPECIAL) as b:
                    for j in range(SLOTS):
                        round_step(g, b, j)
                act.wait_ge(out_stored, g * 32)
                round_special_block(g)
                round_last_block(g)

            e = GROUPS - 1
            relus(e)
            take_root(e, 0)
            normalise(e, 0, of_banks=range(0, 1))
            take_root(e, 1)
            normalise(e, 0, of_banks=range(1, 2))
            normalise(e, 1, of_banks=range(0, 1))

        @block.vector
        def _(dve):
            def subtract_step(g, b, j, rows=P):
                dve.wait_ge(hi_ready, g * COUNTED + b * SLOTS + (j + 1))
                dve.tensor_tensor(lo[0:rows, j, :], raw[0:rows, j, :], hi[0:rows, j, :].bitcast(F32),
                                  ALU.subtract).then_inc(lo_ready, 1)

            def subtract_special_block(g, between=lambda: None):
                subtract_step(g, SPECIAL, 0)
                dve.wait_ge(hi_ready, g * COUNTED + (TAIL_STEP + 1))
                rounded = hi[0:TAIL, TAIL_SLOT, :].bitcast(F32)
                dve.tensor_copy(hi[2 * TAIL:3 * TAIL, TAIL_SLOT, :], rounded)
                dve.tensor_tensor(hi[TAIL:2 * TAIL, TAIL_SLOT, :], raw[0:TAIL, TAIL_SLOT, :],
                                  rounded, ALU.subtract).then_inc(lo_ready, 1)
                between()
                subtract_step(g, SPECIAL, X_SLOT)
                subtract_step(g, SPECIAL, LAST_SLOT)

            def subtract_last_block(g):
                for j in range(LAST_SLOT):
                    subtract_step(g, BLOCKS - 1, j)
                for n, cols in banks():
                    dve.wait_ge(last_hi_ready, g * BANKS + n + 1)
                    dve.tensor_tensor(lo[0:SHORT, LAST_SLOT, cols], raw[0:SHORT, LAST_SLOT, cols],
                                      hi[0:SHORT, LAST_SLOT, cols].bitcast(F32), ALU.subtract
                                      ).then_inc(last_lo_ready, 1)

            def add_bias(q, bank, tiles=BATCH):
                if q is not FIRST_BATCH:
                    dve.wait_ge(h_lo_ready, q)
                dve.wait_ge(h_psum_done, q + 1)
                dve.tensor_tensor(h_sum[:, 0:tiles * HID].rearrange("p (t c) -> p t c", c=HID),
                                  aux[:, bank, 0:tiles * HID].rearrange("p (t c) -> p t c", c=HID),
                                  b_item_all[:, :].unsqueeze(1).to_broadcast([P, tiles, HID]),
                                  ALU.add).then_inc(h_sum_ready, 1)

            def subtract_h(q, tiles=BATCH):
                dve.wait_ge(h_hi_ready, q + 1)
                part = (slice(None), bass.ds(q * BATCH, tiles), slice(None))
                dve.tensor_tensor(h_lo[part].rearrange("p t c -> p (t c)"), h_sum[:, 0:tiles * HID],
                                  h_hi[part].rearrange("p t c -> p (t c)").bitcast(F32),
                                  ALU.subtract).then_inc(h_lo_ready, 1)

            def take_stats(e, n):
                dve.wait_ge(transposed, e * BANKS + n + 1)
                for s in range(n * SUBS_PER_BANK, (n + 1) * SUBS_PER_BANK):
                    users, col = SUB_USERS[s], (s % SUBS_PER_BANK) * P
                    done = dve.bn_stats(stats[0:users, s, :], aux[0:users, n, col:col + HID])
                done.then_inc(stats_taken, 1)

            def await_stats(e, half):
                dve.wait_ge(stats_taken, e * BANKS + (half + 1) * HALF_BANKS)

            def merge_stats(half):
                for s in range(half * HALF_SUBS, (half + 1) * HALF_SUBS):
                    done = dve.bn_aggr(moments[0:SUB_USERS[s], s, :], stats[0:SUB_USERS[s], s, :])
                done.then_inc(merged, 1)

            def make_scale(e, half, between=lambda i: None):
                subs, nth = slice(half * HALF_SUBS, (half + 1) * HALF_SUBS), e * 2 + half + 1
                dve.wait_ge(std_ready, nth)
                dve.reciprocal(guess[:, subs], std[:, subs]).then_inc(guess_ready, 1)
                between(0)
                dve.wait_ge(guess_ready, nth)
                dve.scalar_tensor_tensor(out=check[:, subs], in0=moments[:, subs, 1], scalar=EPS, in1=guess[:, subs],
                                         op0=ALU.add, op1=ALU.mult).then_inc(check_ready, 1)
                dve.wait_ge(check_ready, nth * 3 - 2)
                dve.tensor_tensor(check[:, subs], check[:, subs], guess[:, subs], ALU.mult).then_inc(check_ready, 1)
                between(1)
                dve.wait_ge(check_ready, nth * 3 - 1)
                dve.tensor_scalar(check[:, subs], check[:, subs], -0.5, 1.5, ALU.mult, ALU.add
                                  ).then_inc(check_ready, 1)
                dve.wait_ge(check_ready, nth * 3)
                dve.tensor_tensor(rstd[:, subs], check[:, subs], guess[:, subs], ALU.mult).then_inc(rstd_ready, 1)
                between(2)
                dve.wait_ge(rstd_ready, nth)
                dve.scalar_tensor_tensor(out=shift[:, subs], in0=moments[:, subs, 0], scalar=-1.0, in1=rstd[:, subs],
                                         op0=ALU.mult, op1=ALU.mult).then_inc(shift_ready, 1)
                between(3)

            def add_residual_too(n):
                dve.wait_ge(relu_done, (GROUPS - 1) * BANKS + n + 1)
                cols = banks()[n][1]
                dve.tensor_tensor(res[:, cols], relu[:, cols], res[:, cols], ALU.add).then_inc(y_too_ready, 1)

            def normalise_last_bank():
                n = BANKS - 1
                dve.wait_ge(shift_ready, GROUPS * 2)
                for s in range(n * SUBS_PER_BANK, SUBS):
                    users, col = SUB_USERS[s], (s % SUBS_PER_BANK) * P
                    done = dve.tensor_scalar(norm[0:users, s, :], aux[0:users, n, col:col + HID],
                                             rstd[0:users, s:s + 1], shift[0:users, s:s + 1], ALU.mult, ALU.add)
                done.then_inc(normed_too, 1)

            dve.memset(moments[:, :, :], 1.0).then_inc(fills_ready, 1)
            dve.memset(eps_col[:, :], EPS).then_inc(fills_ready, 1)
            dve.wait_ge(fills_ready, 2)
            dve.wait_ge(w_hi_ready, 1)
            dve.wait_ge(biases_loaded, 32)
            dve.tensor_tensor(h_lo[:, H_TILES, :], w_user[:, :], h_hi[:, H_TILES, :].bitcast(F32),
                              ALU.subtract).then_inc(w_lo_ready, 1)

            def subtract_block_and_h(b, bank):
                for j in range(SLOTS):
                    if j == 0:
                        add_bias(b + 1, bank)
                    if j == SLOTS // 2:
                        subtract_h(b + 1)
                    subtract_step(0, b, j)

            add_bias(FIRST_BATCH, 0)
            subtract_h(FIRST_BATCH)
            with dve.Fori(0, SPECIAL // 2) as pair:
                subtract_block_and_h(pair * 2, 1)
                subtract_block_and_h(pair * 2 + 1, 0)
            add_bias(H_BATCHES - 1, 1, LAST_BATCH)
            subtract_special_block(0, between=lambda: subtract_h(H_BATCHES - 1, LAST_BATCH))
            subtract_last_block(0)

            with dve.Fori(1, GROUPS) as g:
                e = g - 1
                for b in range(WOVEN):
                    if b in STATS_BLOCKS:
                        for n in range(HALF_BANKS):
                            take_stats(e, STATS_BLOCKS.index(b) * HALF_BANKS + n)
                    if b in MERGE_BLOCKS:
                        await_stats(e, MERGE_BLOCKS.index(b))
                        subtract_step(g, b, 0)
                        merge_stats(MERGE_BLOCKS.index(b))
                        for j in range(1, SLOTS):
                            subtract_step(g, b, j)
                    elif b in RSTD_BLOCKS:
                        make_scale(e, RSTD_BLOCKS.index(b), between=lambda j: subtract_step(g, b, j))
                    else:
                        for j in range(SLOTS):
                            subtract_step(g, b, j)
                with dve.Fori(WOVEN, SPECIAL) as b:
                    for j in range(SLOTS):
                        subtract_step(g, b, j)
                subtract_special_block(g)
                subtract_last_block(g)

            e = GROUPS - 1
            add_residual_too(1)
            add_residual_too(2)
            take_stats(e, 0)
            take_stats(e, 1)
            await_stats(e, 0)
            merge_stats(0)
            make_scale(e, 0, between=lambda i: take_stats(e, 2 + i) if i < HALF_BANKS else None)
            await_stats(e, 1)
            merge_stats(1)
            make_scale(e, 1)
            normalise_last_bank()

        @block.tensor
        def _(pe):
            def multiply_h(q):
                chunk = q * BATCH // CHUNK
                if q == 0:
                    pe.wait_ge(item_first_loaded, 16)
                elif q == 1 or q * BATCH % CHUNK == 0:
                    pe.wait_ge(item_loaded[chunk % 2], 16 * (chunk // 2 + 1))
                if q >= 2:
                    pe.wait_ge(h_sum_ready, q - 1)
                for t in range(q * BATCH, min((q + 1) * BATCH, H_TILES)):
                    at = (t - chunk * CHUNK) * P
                    done = pe.matmul(aux[:, q % 2, (t % BATCH) * HID:(t % BATCH + 1) * HID],
                                     stage[:, chunk % 2, at:at + P], w_item[:, :], start=True, stop=True)
                done.then_inc(h_psum_done, 1)

            def multiply(n, j, weights, moving, start=False, stop=False, rows=P):
                return pe.matmul(acc[:, n, 0:WIDTH[n]], weights, moving[0:rows, j, n * BANK:n * BANK + WIDTH[n]],
                                 start=start, stop=stop)

            def multiply_first_step(g):
                pe.wait_ge(lo_ready, g * COUNTED + 1)
                for n in range(BANKS):
                    if g is not FIRST_GROUP:
                        pe.wait_ge(relu_done, g * BANKS + (n - BANKS + 1))
                    multiply(n, 0, h_lo[:, 0, :], hi, start=True)
                    multiply(n, 0, h_hi[:, 0, :], hi)
                    done = multiply(n, 0, h_hi[:, 0, :], lo)
                done.then_inc(step_done, 1)

            def multiply_step(g, k):
                j = k % SLOTS
                if k == TAIL_STEP:
                    pe.wait_ge(lo_ready, g * COUNTED + (k + 1))
                    for n in range(BANKS):
                        done = multiply(n, j, h_tail[:, :], hi, rows=TAIL_ROWS)
                else:
                    tile = k if k < X_STEP else H_TILES if k == X_STEP else k - 1
                    pe.wait_ge(hi_ready, g * COUNTED + (k + 1))
                    for n in range(BANKS):
                        multiply(n, j, h_lo[:, tile, :], hi)
                    for n in range(BANKS):
                        multiply(n, j, h_hi[:, tile, :], hi)
                    pe.wait_ge(lo_ready, g * COUNTED + (k + 1))
                    for n in range(BANKS):
                        done = multiply(n, j, h_hi[:, tile, :], lo)
                done.then_inc(step_done, 1)

            def multiply_last_step(g):
                w_hi, w_lo = h_hi[0:SHORT, H_TILES - 1, :], h_lo[0:SHORT, H_TILES - 1, :]
                for n in range(BANKS):
                    pe.wait_ge(last_lo_ready, g * BANKS + n + 1)
                    multiply(n, LAST_SLOT, w_lo, hi, rows=SHORT)
                    multiply(n, LAST_SLOT, w_hi, hi, rows=SHORT)
                    multiply(n, LAST_SLOT, w_hi, lo, rows=SHORT, stop=True).then_inc(acc_done, 1)

            def transpose_banks(e, last=False):
                for n in range(BANKS):
                    if last and 0 < n < BANKS - 1:
                        pe.wait_ge(y_too_ready, n)
                    elif last and n == BANKS - 1:
                        pe.wait_ge(y_ready, e * BANKS + 2)
                    else:
                        pe.wait_ge(y_ready, e * BANKS + n + 1)
                    for s in range(n * SUBS_PER_BANK, (n + 1) * SUBS_PER_BANK):
                        users, col = SUB_USERS[s], (s % SUBS_PER_BANK) * P
                        done = pe.transpose(aux[0:users, n, col:col + HID], res[:, s * P:s * P + users], ident[:, :])
                    done.then_inc(transposed, 1)

            pe.wait_ge(weights_loaded, 32)
            pe.wait_ge(ident_ready, 2)
            multiply_h(0)
            multiply_h(1)
            pe.wait_ge(w_lo_ready, 1)
            for k in range(LAST_STEP):
                if k == TAIL_STEP:
                    pe.wait_ge(h_tail_ready, 1)
                if k % SLOTS == 0:
                    if k // SLOTS + 2 < H_BATCHES:
                        multiply_h(k // SLOTS + 2)
                    pe.wait_ge(h_lo_ready, k // SLOTS + 1)
                if k == 0:
                    multiply_first_step(FIRST_GROUP)
                else:
                    multiply_step(FIRST_GROUP, k)
            multiply_last_step(FIRST_GROUP)

            with pe.Fori(1, GROUPS) as g:
                multiply_first_step(g)
                for k in range(1, LAST_STEP):
                    if k == SLOTS:
                        transpose_banks(g - 1)
                    multiply_step(g, k)
                multiply_last_step(g)
            transpose_banks(GROUPS - 1, last=True)


def kernel(x, adj, L0_gnn_item_feat, L0_gnn_W_item, L0_gnn_b_item, L0_gnn_W_user, L0_gnn_b_user):
    import concourse.bacc as bacc
    from concourse.bass_utils import run_bass_kernel_spmd

    def by_group(a_T):
        rows = a_T.shape[0]
        grouped = np.zeros((GROUPS, rows, PITCH), a_T.dtype)
        grouped[:, :, :GROUP_USERS] = a_T.reshape(rows, GROUPS, GROUP_USERS).transpose(1, 0, 2)
        return grouped.reshape(GROUPS * rows, PITCH)

    adj_T = np.asarray(adj).T
    items = np.asarray(L0_gnn_item_feat).T
    item_T = np.zeros((HID, H_TILES * P), items.dtype)
    before = TAIL_STEP * P
    item_T[:, :before] = items[:, :before]
    item_T[:, before:before + TAIL] = items[:, ITEMS - TAIL:]
    item_T[:, before + P:before + P + (ITEMS - TAIL - before)] = items[:, before:ITEMS - TAIL]
    arrays = {
        "adj_T": by_group(adj_T),
        "x_T": by_group(np.ascontiguousarray(np.asarray(x).T)),
        "item_T": item_T,
        "w_item_T": np.ascontiguousarray(np.asarray(L0_gnn_W_item).T),
        "w_user_T": np.ascontiguousarray(np.asarray(L0_gnn_W_user).T),
        "b_item": np.asarray(L0_gnn_b_item),
        "b_user": np.asarray(L0_gnn_b_user).reshape(HID, 1),
    }
    nc = bacc.Bacc("TRN2", target_bir_lowering=False, num_devices=1)
    ins = [nc.dram_tensor(name, a.shape, mybir.dt.from_np(a.dtype), kind="ExternalInput").ap()
           for name, a in arrays.items()]
    out = nc.dram_tensor("out", (USERS, HID), F32, kind="ExternalOutput").ap()
    build(nc, *ins, out)
    result = run_bass_kernel_spmd(nc, [arrays], core_ids=[0])
    return result.results[0]["out"]
```
